# Optimizing a Trainium2 kernel written in Bass

```python
import numpy as np
import jax
import jax.numpy as jnp

def _softmax(x, axis=-1):
    return jax.nn.softmax(x, axis=axis)
def _gelu(x):
    return jax.nn.gelu(x, approximate=True)
def _silu(x):
    return jax.nn.silu(x)
def _sigmoid(x):
    return jax.nn.sigmoid(x)
def _layernorm(x, axis=-1, eps=1e-5):
    m = jnp.mean(x, axis=axis, keepdims=True)
    v = jnp.var(x, axis=axis, keepdims=True)
    return (x - m) / jnp.sqrt(v + eps)
def _scatter_add(tgt, idx, src, axis=0):
    return tgt.at[idx].add(src)
def _segment_sum(src, seg, n):
    return jax.ops.segment_sum(src, seg, n)

kernel_name = 'mk_conv_preact_d2_conv_nchw64_c52fef'

def setup_inputs(seed: int = 0):
    np.random.seed(seed)
    _w = jnp.asarray
    def _rec_inputs():
        import jax
        import jax.numpy as jnp
        _gk = jax.random.key(seed)
        x = -8.268e-05 + 0.9999 * jax.random.normal(jax.random.fold_in(_gk, 1), (64, 64, 112, 112), jnp.float32)
        return x
    x = _rec_inputs()
    def _L0_conv_setup():
        import jax, jax.numpy as jnp
        import numpy as np
        import math
        B, C_IN, C_OUT, H, W = (64, 64, 64, 112, 112)
        A_MAX, T = (3, 8)

        def _spiral_offsets(c_in, a_max, t):
            offs = []
            for c in range(c_in):
                if a_max == 0:
                    dh, dw = (0, 0)
                else:
                    if 0 <= c < c_in / 2:
                        ac = math.floor(2 * a_max / c_in * c)
                    else:
                        ac = math.floor(2 * a_max - 2 * a_max / c_in * c)
                    angle = c * 2 * math.pi / t
                    dh = round(ac * math.cos(angle))
                    dw = round(ac * math.sin(angle))
                offs.append((dh, dw))
            return np.asarray(offs, dtype=np.int32)
        key = jax.random.key(seed)
        kx, kw = jax.random.split(key)
        x = jax.random.normal(kx, (B, C_IN, H, W), dtype=jnp.float32)
        weight = jax.random.normal(kw, (C_IN, C_OUT), dtype=jnp.float32)
        bias = jnp.zeros((C_OUT,), dtype=jnp.float32)
        offsets = jnp.asarray(_spiral_offsets(C_IN, A_MAX, T))
        return {'x': x, 'weight': weight, 'bias': bias, 'offsets': offsets}
    _L0_conv_all = _L0_conv_setup()
    _L0_conv_in = {k: v for k, v in _L0_conv_all.items() if k in ('weight', 'bias', 'offsets', )}
    del _L0_conv_all

    def _L1_conv_setup():
        import jax, jax.numpy as jnp
        import numpy as np
        C_IN = 64
        C_OUT = 64
        GRP_N = 8
        OVERLAP = 4
        G = C_IN // GRP_N
        STEP = G - OVERLAP
        B, H, W = (32, 128, 128)

        def _expand_weights(weights):
            o = jnp.arange(C_OUT)[:, None]
            j = jnp.arange(G)[None, :]
            idx = (o * STEP + j) % C_IN
            w_full = jnp.zeros((C_OUT, C_IN), dtype=weights.dtype)
            w_full = w_full.at[jnp.broadcast_to(o, idx.shape), idx].add(weights)
            return w_full
        key = jax.random.key(seed)
        k1, k2 = jax.random.split(key)
        x = jax.random.normal(k1, (B, C_IN, H, W), dtype=jnp.float32)
        stdv = 1.0 / np.sqrt(G)
        weights = jax.random.uniform(k2, (C_OUT, G), dtype=jnp.float32, minval=-stdv, maxval=stdv)
        return {'x': x, 'weights': weights}
    _L1_conv_all = _L1_conv_setup()
    _L1_conv_in = {k: v for k, v in _L1_conv_all.items() if k in ('weights', )}
    del _L1_conv_all

    return {
        "x": x,
        "L0_conv_weight": _L0_conv_in["weight"],
        "L0_conv_bias": _L0_conv_in["bias"],
        "L0_conv_offsets": _L0_conv_in["offsets"],
        "L1_conv_weights": _L1_conv_in["weights"],
    }

def reference(x, L0_conv_weight, L0_conv_bias, L0_conv_offsets, L1_conv_weights):
    import jax
    import jax.numpy as jnp
    def _L0_conv_ref(x, weight, bias, offsets):
        import jax, jax.numpy as jnp
        import numpy as np
        import math
        B, C_IN, C_OUT, H, W = (64, 64, 64, 112, 112)
        A_MAX, T = (3, 8)

        def _spiral_offsets(c_in, a_max, t):
            offs = []
            for c in range(c_in):
                if a_max == 0:
                    dh, dw = (0, 0)
                else:
                    if 0 <= c < c_in / 2:
                        ac = math.floor(2 * a_max / c_in * c)
                    else:
                        ac = math.floor(2 * a_max - 2 * a_max / c_in * c)
                    angle = c * 2 * math.pi / t
                    dh = round(ac * math.cos(angle))
                    dw = round(ac * math.sin(angle))
                offs.append((dh, dw))
            return np.asarray(offs, dtype=np.int32)
        P = A_MAX
        b, c, h, w = x.shape
        x_padded = jnp.pad(x, ((0, 0), (0, 0), (P, P), (P, P)))
        h_idx = (P + offsets[:, 0])[:, None] + jnp.arange(h)[None, :]
        w_idx = (P + offsets[:, 1])[:, None] + jnp.arange(w)[None, :]
        c_idx = jnp.arange(c)
        sampled = x_padded[:, c_idx[:, None, None], h_idx[:, :, None], w_idx[:, None, :]]
        out = jnp.einsum('bchw,co->bohw', sampled, weight) + bias[None, :, None, None]
        return out

    def _L1_conv_ref(x, weights):
        import jax, jax.numpy as jnp
        import numpy as np
        C_IN = 64
        C_OUT = 64
        GRP_N = 8
        OVERLAP = 4
        G = C_IN // GRP_N
        STEP = G - OVERLAP
        B, H, W = (32, 128, 128)

        def _expand_weights(weights):
            o = jnp.arange(C_OUT)[:, None]
            j = jnp.arange(G)[None, :]
            idx = (o * STEP + j) % C_IN
            w_full = jnp.zeros((C_OUT, C_IN), dtype=weights.dtype)
            w_full = w_full.at[jnp.broadcast_to(o, idx.shape), idx].add(weights)
            return w_full
        w_full = _expand_weights(weights)
        return jnp.einsum('oc,bchw->bohw', w_full, x)

    def _gn(v, G=32, eps=1e-5):
        B_, C_, H_, W_ = v.shape
        g = v.reshape(B_, G, C_ // G, H_, W_)
        m = jnp.mean(g, axis=(2, 3, 4), keepdims=True)
        s = jnp.var(g, axis=(2, 3, 4), keepdims=True)
        return ((g - m) / jnp.sqrt(s + eps)).reshape(v.shape)

    def _ln_c(v, eps=1e-6):
        m = jnp.mean(v, axis=1, keepdims=True)
        s = jnp.var(v, axis=1, keepdims=True)
        return (v - m) / jnp.sqrt(s + eps)

    def _ln_t(v, eps=1e-5):
        m = jnp.mean(v, axis=-1, keepdims=True)
        s = jnp.var(v, axis=-1, keepdims=True)
        return (v - m) / jnp.sqrt(s + eps)

    def _to_tokens(v):
        B_, C_, H_, W_ = v.shape
        return v.reshape(B_, C_, H_ * W_).transpose(0, 2, 1)
    def _from_tokens(t, like):
        B_, C_, H_, W_ = like.shape
        return t.transpose(0, 2, 1).reshape(B_, C_, H_, W_)

    x = x + _L0_conv_ref(_gn(x), L0_conv_weight, L0_conv_bias, L0_conv_offsets)
    x = x + _L1_conv_ref(_gn(x), L1_conv_weights)
    return x


_drawn_inputs = setup_inputs


def setup_inputs(seed=0):
    import zlib

    import numpy as np

    out = dict(_drawn_inputs(seed))
    spreads = {'L0_conv_bias': (0.0, 0.679)}
    factors = {}
    for name, (base, spread) in spreads.items():
        noise = np.random.default_rng([zlib.crc32(name.encode()), seed]).standard_normal(out[name].shape)
        drawn = base * np.exp(spread * noise) if base else spread * noise
        out[name] = jnp.asarray(drawn.astype(out[name].dtype))
    for name, factor in factors.items():
        out[name] = (out[name] * factor).astype(out[name].dtype)
    return out
```

```python
from contextlib import ExitStack

import concourse.bass as bass
from concourse import mybir
import numpy as np

P = 128
C = 64
BATCH, H, W = 64, 112, 112
HW = H * W
PAIRS = BATCH * C // P
PAIR_ELEMS = P * HW
PAD = 3
HALO = PAD * W + PAD
GROUP_ROWS = 8
BANK_COLS = GROUP_ROWS // 2 * W
GROUP = GROUP_ROWS * W
GROUPS = HW // GROUP
CHUNK = 2 * GROUP
CHUNK_ROWS = CHUNK // W
CHUNKS = HW // CHUNK
SCRATCH = CHUNK + 2 * HALO
LOW_BITS = 8
UNIT = 1 << LOW_BITS
SHIFT_BIAS = 2 * UNIT
BUFS = 3
SLOTS = 3
LAG = 18
FIRST = 2
ROUNDS = (PAIRS - FIRST - 1) // BUFS
LOOP_END = FIRST + ROUNDS * BUFS
EPS = 1e-5
assert HW % UNIT == 0 and CHUNK % UNIT == 0 and FIRST * GROUPS > LAG + 3 and GROUPS % 2 == 0


LINKS_PER_STEP = 22


class Tally:

    def __init__(self):
        self.count = 0
        self.per_step = 0
        self.inner = 0
        self.step = None

    def enter(self, steps, per_step):
        self.step, self.per_step, self.inner = steps, per_step, 0

    def leave(self, steps):
        assert self.inner == self.per_step, (self.inner, self.per_step)
        self.count += steps * self.per_step
        self.step, self.inner = None, 0

    def next(self):
        if self.step is None:
            self.count += 1
            return self.count
        self.inner += 1
        return self.step * self.per_step + (self.count + self.inner)


def build(nc, x, w0, b0, offsets, w1, consts, out):
    f32, i32 = mybir.dt.float32, mybir.dt.int32
    ALU, ACT, AX = mybir.AluOpType, mybir.ActivationFunctionType, mybir.AxisListType.X

    x_pairs = x.rearrange("b c h w -> (b c) (h w)").rearrange("(n p) f -> n p f", p=P)
    out_pairs = out.rearrange("b c h w -> (b c) (h w)").rearrange("(n p) f -> n p f", p=P)
    x_flat = x.rearrange("b c h w -> (b c h w)").rearrange("(n o) -> n o", o=1)
    head = nc.dram_tensor("head_chunk", (P, SCRATCH), f32, kind="Internal").ap()
    tail = nc.dram_tensor("tail_chunk", (P, SCRATCH), f32, kind="Internal").ap()
    head_flat = head.rearrange("p f -> (p f)").rearrange("(n o) -> n o", o=1)
    tail_flat = tail.rearrange("p f -> (p f)").rearrange("(n o) -> n o", o=1)
    w1_expanded = nc.dram_tensor("w1_expanded", (C, C), f32, kind="Internal").ap()

    with ExitStack() as ctx:
        def sb(name, shape, dt=f32):
            return ctx.enter_context(nc.sbuf_tensor(name, shape, dt))

        def sem(name):
            return ctx.enter_context(nc.semaphore(name))

        images = [sb(f"images{b}", [P, HW]) for b in range(BUFS)]
        shifted = sb("shifted", [P, HW])
        square_out = sb("square_out", [P, GROUP])
        const_sb = sb("const_sb", [P, 3, P])
        group_mean_w, group_diff_w, identity = const_sb[:, 0, :], const_sb[:, 1, :], const_sb[:, 2, :]
        w0_blocks = sb("w0_blocks", [P, P])
        w1_blocks = sb("w1_blocks", [P, P])
        w0_scaled = sb("w0_scaled", [P, BUFS, P])
        w1_scaled = sb("w1_scaled", [P, BUFS, P])
        bias_in = sb("bias_in", [P, 1])
        bias0 = sb("bias0", [P, BUFS, 1])
        bias1 = sb("bias1", [P, BUFS, 1])
        shift_guess = sb("shift_guess", [P, BUFS, 1])
        bn = sb("bn", [P, GROUPS * 2, 6])
        mean_var = sb("mean_var", [P, 2, 2])
        x1_sums = sb("x1_sums", [P, BUFS, GROUPS])
        x1_squares = sb("x1_squares", [P, BUFS, GROUPS])
        small = sb("small", [P, 2, 8])
        group_mean0 = sb("group_mean0", [P, BUFS, 1])
        offs = sb("offs", [P, 2], i32)
        offs_f = sb("offs_f", [P, 2])
        flat_shift = sb("flat_shift", [P, 2])
        shift_int = sb("shift_int", [P, 3], i32)
        high = sb("high", [P, CHUNKS], i32)
        scratch_index = sb("scratch_index", [P, 1], i32)
        index = sb("index", [P, BUFS, CHUNKS], i32)
        col_mask = sb("col_mask", [P, 2, PAD], i32)
        row_mask = sb("row_mask", [P, 2, PAD], i32)

        slots = [ctx.enter_context(nc.psum_tensor(f"slot{s}", [P, 2, 512], f32)) for s in range(SLOTS)]
        stats_ps = ctx.enter_context(nc.psum_tensor("stats_ps", [P, 512], f32))
        mean_ps = ctx.enter_context(nc.psum_tensor("mean_ps", [P, 512], f32))

        consts_loaded = sem("consts_loaded")
        offsets_loaded = sem("offsets_loaded")
        blocks_zeroed = sem("blocks_zeroed")
        w1_zeroed = sem("w1_zeroed")
        w1_spread = sem("w1_spread")
        w1_loaded = sem("w1_loaded")
        counted = sem("counted")
        head_written, tail_written = sem("head_written"), sem("tail_written")
        x_loaded = [[sem(f"x_loaded{b}_{j}") for j in range(CHUNKS)] for b in range(BUFS)]
        stored = [[sem(f"stored{b}_{j}") for j in range(CHUNKS)] for b in range(BUFS)]
        gathered = [sem(f"gathered{j}") for j in range(CHUNKS)]
        index_ready = sem("index_ready")
        edges_fixed = sem("edges_fixed")
        l0_filled, l1_filled = sem("l0_filled"), sem("l1_filled")
        l0_added, l1_evacuated = sem("l0_added"), sem("l1_evacuated")
        squares_summed = sem("squares_summed")
        moments_ready = sem("moments_ready")
        stats_ready = sem("stats_ready")
        variance_ready = sem("variance_ready")
        root_ready = sem("root_ready")
        weights_ready = sem("weights_ready")
        mean_ready = sem("mean_ready")
        bias_ready = sem("bias_ready")
        masks_ready = sem("masks_ready")
        dve_step = sem("dve_step")

        dve_passed, pool_passed, sp_passed = sem("dve_passed"), sem("pool_passed"), sem("sp_passed")

        def wait_apart(eng, semaphore, value, passed):
            eng.wait_ge(semaphore, value)
            eng.sem_inc(passed, 1)

        def chunk(t, j):
            return t[:, j * CHUNK:(j + 1) * CHUNK]

        def group(t, g):
            return t[:, g * GROUP:(g + 1) * GROUP]

        def group_banks(t, g):
            return group(t, g).rearrange("p (k f) -> p k f", k=2)

        def x_chain(n):
            return 0 if isinstance(n, int) and n == 0 else n * 2 - 1

        def x1_chain(n):
            return 2 * PAIRS - 1 if isinstance(n, int) and n == PAIRS - 1 else n * 2 + 2

        def in_steps(eng, step, tally=None, per_step=0):
            for n in range(FIRST):
                step(n, n % BUFS, n // BUFS + 1)
            with eng.Fori(0, ROUNDS) as i:
                for u in range(BUFS):
                    if tally is not None:
                        tally.enter(i * BUFS + u, per_step)
                    n = FIRST + u
                    step(i * BUFS + n, n % BUFS, i + (n // BUFS + 1))
                    if tally is not None:
                        assert tally.inner == per_step, tally.inner
            if tally is not None:
                tally.leave(ROUNDS * BUFS)
            for n in range(LOOP_END, PAIRS):
                step(n, n % BUFS, n // BUFS + 1)

        def behind(n, b, g, do):
            back, at = divmod(g - LAG, GROUPS)
            if isinstance(n, int) and n + back < 0:
                return
            do(n + back, (b + back) % BUFS, at, layer1_slot(n, b, g))

        def layer0_slot(n, b, g):
            if isinstance(n, int) and n * GROUPS + g < LAG:
                return (n * GROUPS + g) % SLOTS
            return (2 * (b * GROUPS + g) - LAG) % SLOTS

        def layer1_slot(n, b, g):
            return (layer0_slot(n, b, g) + 1) % SLOTS

        def tail_slot(t):
            return (2 * PAIRS * GROUPS - LAG + t - PAIRS * GROUPS) % SLOTS

        block = ctx.enter_context(nc.Block())

        @block.sync
        def _(sp):
            sp.dma_start(head[:, HALO:SCRATCH], x_pairs[0, :, 0:CHUNK + HALO]).then_inc(head_written, 16)
            sp.dma_start(head[:, 0:HALO], x_pairs[0, :, 0:HALO]).then_inc(head_written, 16)

            def load(n, b, j):
                sp.dma_start(chunk(images[b], j), x_pairs[n, :, j * CHUNK:(j + 1) * CHUNK]) \
                    .then_inc(x_loaded[b][j], 16)

            def store(m, b, j):
                wait_apart(sp, l1_evacuated, m * GROUPS + (2 * j + 2), sp_passed)
                sp.dma_start(out_pairs[m, :, j * CHUNK:(j + 1) * CHUNK], chunk(images[b], j)) \
                    .then_inc(stored[b][j], 16)

            def reload(m, b, j, uses):
                wait_apart(sp, stored[b][j], uses * 16, sp_passed)
                load(m + BUFS, b, j)

            for j in range(CHUNKS):
                load(0, 0, j)
            sp.wait_ge(gathered[2], 16)
            for j in range(CHUNKS):
                load(1, 1, j)
            for j in range(CHUNKS):
                sp.wait_ge(l0_filled, 2 * j + 2)
                load(2, 2, j)
            sp.dma_start(tail[:, 0:CHUNK + HALO], x_pairs[PAIRS - 1, :, HW - CHUNK - HALO:HW]) \
                .then_inc(tail_written, 16)
            sp.dma_start(tail[:, CHUNK + HALO:SCRATCH], x_pairs[PAIRS - 1, :, 0:HALO]).then_inc(tail_written, 16)

            def store_pair(m, b, uses, uses_before, reload_last, reload_this):
                for j in range(CHUNKS):
                    store(m, b, j)
                    if j == 0 and reload_last:
                        reload(m - 1, (b - 1) % BUFS, CHUNKS - 1, uses_before)
                    elif j > 0 and reload_this:
                        reload(m, b, j - 1, uses)

            rounds = (PAIRS - BUFS) // BUFS
            store_pair(0, 0, 1, 0, False, True)
            store_pair(1, 1, 1, 1, True, True)
            store_pair(2, 2, 1, 1, True, True)
            with sp.Fori(1, rounds) as i:
                for b in range(BUFS):
                    store_pair(i * BUFS + b, b, i + 1, i + (1 if b else 0), True, True)
            for m in range(rounds * BUFS, PAIRS):
                store_pair(m, m % BUFS, m // BUFS + 1, (m - 1) // BUFS + 1, m - 1 + BUFS < PAIRS, m + BUFS < PAIRS)
            for b in range(BUFS):
                for j in range(CHUNKS):
                    sp.wait_ge(stored[b][j], 16 * len(range(b, PAIRS, BUFS)))

        @block.gpsimd
        def _(pool):
            nc.gpsimd.iota(high[:], [[CHUNK // UNIT, CHUNKS]], base=0, channel_multiplier=HW // UNIT)
            nc.gpsimd.iota(scratch_index[:], [[0, 1]], base=HALO, channel_multiplier=SCRATCH).then_inc(counted, 1)

            def gather(source, at, j):
                nc.gpsimd.indirect_dma_start(
                    chunk(shifted, j), None, source,
                    bass.IndirectOffsetOnAxis(ap=at, axis=0)).then_inc(gathered[j], 16)

            pool.wait_ge(index_ready, 1)
            pool.wait_ge(head_written, 32)
            gather(head_flat, scratch_index[:, 0:1], 0)
            for j in range(1, CHUNKS):
                gather(x_flat, index[:, 0, j:j + 1], j)

            def gather_pair(n, b, last=False):
                pool.wait_ge(index_ready, n + 1)
                for j in range(CHUNKS):
                    wait_apart(pool, l0_filled, n * GROUPS + (2 * j + 2 - GROUPS), pool_passed)
                    if last and j == CHUNKS - 1:
                        pool.wait_ge(tail_written, 32)
                        gather(tail_flat, scratch_index[:, 0:1], j)
                    else:
                        gather(x_flat, index[:, b, j:j + 1], j)

            rounds = (PAIRS - 2) // BUFS
            with pool.Fori(0, rounds) as i:
                for u in range(BUFS):
                    gather_pair(i * BUFS + (1 + u), (1 + u) % BUFS)
            for n in range(1 + rounds * BUFS, PAIRS):
                gather_pair(n, n % BUFS, n == PAIRS - 1)

        @block.scalar
        def _(act):
            for half in range(2):
                act.dma_start(offs[half * C:(half + 1) * C, :], offsets[:, :]).then_inc(offsets_loaded, 16)
            act.dma_start(const_sb[:], consts.rearrange("k p m -> p k m")).then_inc(consts_loaded, 16)
            act.wait_ge(blocks_zeroed, 1)
            for half in range(2):
                here = slice(half * C, (half + 1) * C)
                act.dma_start(bias_in[here, :], b0.rearrange("(c o) -> c o", o=1)).then_inc(consts_loaded, 16)
                act.dma_start(w0_blocks[here, here], w0[:, :]).then_inc(consts_loaded, 16)
            act.dma_start(w1_expanded[:, :], w1_blocks[0:C, 0:C]).then_inc(w1_zeroed, 16)

            def spread_w1():
                taps = w1.shape[1]
                stride = taps // 2
                turn = C // stride
                w1_taps = w1.rearrange("(q r) j -> r j q", r=turn)
                spread = w1_expanded.rearrange("c (q r) -> r c q", r=turn)
                act.wait_ge(w1_zeroed, 16)
                with nc.allow_non_contiguous_dma(reason="single weights, once"):
                    for r in range(turn):
                        inside = min(taps, C - stride * r)
                        act.dma_start(spread[r, stride * r:stride * r + inside, :], w1_taps[r, 0:inside, :]) \
                            .then_inc(w1_spread, 16)
                        if inside < taps:
                            act.dma_start(spread[r, 0:taps - inside, :], w1_taps[r, inside:taps, :]) \
                                .then_inc(w1_spread, 16)
                return turn + 1

            def load_w1(spreads):
                act.wait_ge(w1_spread, 16 * spreads)
                for half in range(2):
                    here = slice(half * C, (half + 1) * C)
                    act.dma_start(w1_blocks[here, here], w1_expanded[:, :]).then_inc(w1_loaded, 16)

            def square(n, b, g):
                act.wait_ge(l0_added, n * GROUPS + (g + 1))
                if not (isinstance(n, int) and n == 0 and g == 0):
                    act.wait_ge(squares_summed, n * GROUPS + g)
                nc.scalar.activation(square_out[:], group(images[b], g), ACT.Square, bias=shift_guess[:, b, :],
                                     accum_out=x1_squares[:, b, g:g + 1]).then_inc(squares_summed, 1)

            def layer1(m, b, g, slot):
                if g == 0:
                    act.wait_ge(bias_ready, x1_chain(m) + 1)
                act.wait_ge(l1_filled, m * GROUPS + (g + 1))
                nc.scalar.activation(group_banks(images[b], g), slots[slot][:, :, 0:BANK_COLS], ACT.Identity,
                                     bias=bias1[:, b, :]).then_inc(l1_evacuated, 1)

            def root(number, layer):
                act.wait_ge(variance_ready, number + 1)
                nc.scalar.activation(small[:, layer, 4:5], small[:, layer, 3:4], ACT.Sqrt).then_inc(root_ready, 1)

            root(0, 0)
            spreads = spread_w1()

            def step(n, b, uses):
                for g in range(GROUPS):
                    if g > 0:
                        square(n, b, g - 1)
                    elif not (isinstance(n, int) and n == 0):
                        square(n - 1, (b - 1) % BUFS, GROUPS - 1)
                    behind(n, b, g, layer1)
                    if g == GROUPS - 2 and isinstance(n, int) and n == 0:
                        load_w1(spreads)
                    if g == 1 and not (isinstance(n, int) and n == 0):
                        root(x1_chain(n - 1), 1)
                    if g == 11 and not (isinstance(n, int) and n == PAIRS - 1):
                        root(x_chain(n + 1), 0)

            in_steps(act, step)
            square(PAIRS - 1, (PAIRS - 1) % BUFS, GROUPS - 1)
            for t in range(PAIRS * GROUPS, PAIRS * GROUPS + LAG):
                if t == PAIRS * GROUPS + 1:
                    root(x1_chain(PAIRS - 1), 1)
                m, g = divmod(t - LAG, GROUPS)
                layer1(m, m % BUFS, g, tail_slot(t))

        @block.vector
        def _(dve):
            link = Tally()

            def then(ins):
                value = link.next()
                ins.then_inc(dve_step, 1)
                dve.wait_ge(dve_step, value)

            V = nc.vector
            V.memset(w0_blocks[:], 0.0)
            V.memset(w1_blocks[:], 0.0).then_inc(blocks_zeroed, 1)

            dve.wait_ge(offsets_loaded, 32)
            then(V.tensor_copy(offs_f[:], offs[:]))
            then(V.tensor_scalar(flat_shift[:, 0:1], offs_f[:, 0:1], float(W), float(SHIFT_BIAS), ALU.mult, ALU.add))
            then(V.tensor_tensor(shift_int[:, 0:1], flat_shift[:, 0:1], offs_f[:, 1:2], ALU.add))
            then(V.tensor_scalar(shift_int[:, 1:2], shift_int[:, 0:1], UNIT - 1, None, ALU.bitwise_and))
            then(V.tensor_scalar(shift_int[:, 2:3], shift_int[:, 0:1], LOW_BITS, None, ALU.logical_shift_right))
            dve.wait_ge(counted, 1)
            then(V.tensor_scalar(high[:], high[:], shift_int[:, 2:3], float(-(SHIFT_BIAS // UNIT)),
                                 ALU.add, ALU.add))
            then(V.tensor_scalar(scratch_index[:], scratch_index[:], shift_int[:, 0:1], float(-SHIFT_BIAS),
                                 ALU.add, ALU.add))

            def indices(b):
                V.tensor_scalar(index[:, b, :], high[:], LOW_BITS, shift_int[:, 1:2],
                                ALU.logical_shift_left, ALU.bitwise_or).then_inc(index_ready, 1)

            def next_pair():
                then(V.tensor_scalar(high[:], high[:], float(PAIR_ELEMS // UNIT), None, ALU.add))

            indices(0)
            next_pair()
            indices(1)
            for axis, mask in ((0, row_mask), (1, col_mask)):
                for k in range(PAD):
                    V.tensor_scalar(mask[:, 0, k:k + 1], offs_f[:, axis:axis + 1], float(k), 0.0,
                                    ALU.add, ALU.is_lt)
                    last = V.tensor_scalar(mask[:, 1, k:k + 1], offs_f[:, axis:axis + 1], float(k), float(PAD - 1),
                                           ALU.add, ALU.is_gt)
            last.then_inc(masks_ready, 1)

            def x_stats(b, uses, k):
                if k % 4 == 0:
                    dve.wait_ge(x_loaded[b][k // 4], uses * 16)
                return V.bn_stats(bn[:, k, :], images[b][:, k * BANK_COLS:(k + 1) * BANK_COLS])

            def x_moments(layer=0):
                V.bn_aggr(mean_var[:, 0, :], bn[:].rearrange("p k s -> p (k s)")).then_inc(moments_ready, 1)

            def x1_moments(n, b):
                s = small[:, 1, :]
                dve.wait_ge(squares_summed, n * GROUPS + GROUPS)
                then(V.reduce_sum(s[:, 0:1], x1_sums[:, b, :], AX))
                then(V.reduce_sum(s[:, 1:2], x1_squares[:, b, :], AX))
                then(V.tensor_scalar(mean_var[:, 1, 0:1], s[:, 0:1], 1.0 / HW, None, ALU.mult))
                then(V.tensor_tensor(s[:, 2:3], mean_var[:, 1, 0:1], shift_guess[:, b, :], ALU.add))
                then(V.tensor_tensor(s[:, 2:3], s[:, 2:3], s[:, 2:3], ALU.mult))
                V.scalar_tensor_tensor(mean_var[:, 1, 1:2], s[:, 1:2], 1.0 / HW, s[:, 2:3],
                                       ALU.mult, ALU.subtract).then_inc(moments_ready, 1)

            def variance(number, layer, b):
                s = small[:, layer, :]
                dve.wait_ge(stats_ready, number + 1)
                then(V.tensor_copy(s[:, 0:3], stats_ps[:, 0:3]))
                if layer == 0:
                    V.tensor_copy(group_mean0[:, b, :], s[:, 0:1])
                    then(V.scalar_tensor_tensor(shift_guess[:, b, :], mean_var[:, 0, 0:1], -1.0, bias_in[:],
                                                ALU.mult, ALU.subtract))
                then(V.tensor_scalar(s[:, 7:8], s[:, 2:3], s[:, 2:3], EPS, ALU.mult, ALU.add))
                ins = V.tensor_tensor(s[:, 3:4], s[:, 7:8], s[:, 1:2], ALU.add)
                ins.then_inc(variance_ready, 1)

            def weights(number, layer, b):
                s = small[:, layer, :]
                dve.wait_ge(root_ready, number + 1)
                then(V.reciprocal(s[:, 5:6], s[:, 4:5]))
                then(V.scalar_tensor_tensor(s[:, 6:7], s[:, 5:6], s[:, 3:4], s[:, 5:6], ALU.mult, ALU.mult))
                then(V.tensor_scalar(s[:, 6:7], s[:, 6:7], -0.5, 1.5, ALU.mult, ALU.add))
                then(V.tensor_tensor(s[:, 7:8], s[:, 5:6], s[:, 6:7], ALU.mult))
                if layer == 0:
                    V.tensor_scalar(w0_scaled[:, b, :], w0_blocks[:], s[:, 7:8], None, ALU.mult) \
                        .then_inc(weights_ready, 1)
                else:
                    V.scalar_tensor_tensor(w1_scaled[:, b, :], w1_blocks[:], s[:, 7:8], identity,
                                           ALU.mult, ALU.add).then_inc(weights_ready, 1)

            def bias(number, layer, b):
                dve.wait_ge(mean_ready, number + 1)
                if layer == 0:
                    ins = V.tensor_tensor(bias0[:, b, :], bias_in[:], mean_ps[:, 0:1], ALU.subtract)
                else:
                    ins = V.tensor_tensor(bias1[:, b, :], small[:, 1, 0:1], mean_ps[:, 0:1], ALU.subtract)
                ins.then_inc(bias_ready, 1)
                dve.wait_ge(bias_ready, number + 1)

            def edge(n, b, j):
                wait_apart(dve, gathered[j], n * 16 + 16, dve_passed)
                mean = group_mean0[:, b, :]
                if j == 0 or j == CHUNKS - 1:
                    side = 0 if j == 0 else 1
                    at = 0 if j == 0 else HW - PAD * W
                    rows = shifted[:, at:at + PAD * W].rearrange("p (h w) -> p h w", w=W)
                    value = link.next()
                    V.copy_predicated(rows, row_mask[:, side, :].unsqueeze(2).to_broadcast([P, PAD, W]),
                                      mean.unsqueeze(2).to_broadcast([P, PAD, W])).then_inc(dve_step, 1)
                    wait_apart(dve, dve_step, value, dve_passed)
                image = chunk(shifted, j).rearrange("p (h w) -> p h w", w=W)
                for side, at in ((0, 0), (1, W - PAD)):
                    last = V.copy_predicated(
                        image[:, :, at:at + PAD],
                        col_mask[:, side, :].unsqueeze(1).to_broadcast([P, CHUNK_ROWS, PAD]),
                        mean.unsqueeze(2).to_broadcast([P, CHUNK_ROWS, PAD]))
                last.then_inc(edges_fixed, 1)

            def layer0(n, b, g):
                dve.wait_ge(l0_filled, n * GROUPS + (g + 1))
                V.scalar_tensor_tensor(group_banks(images[b], g), slots[layer0_slot(n, b, g)][:, :, 0:BANK_COLS],
                                       bias0[:, b, :], group_banks(images[b], g), ALU.add, ALU.add,
                                       accum_out=x1_sums[:, b, g:g + 1]).then_inc(l0_added, 1)

            dve.wait_ge(masks_ready, 1)
            for k in range(2 * GROUPS):
                ins = x_stats(0, 1, k)
            then(ins)
            dve.wait_ge(consts_loaded, 16 * 5)
            x_moments()
            dve.wait_ge(moments_ready, 1)
            variance(0, 0, 0)
            weights(0, 0, 0)
            edge(0, 0, 0)
            bias(0, 0, 0)
            edge(0, 0, 1)
            def step(n, b, uses):
                whole = isinstance(n, int)
                has_x1, has_next = not whole or n > 0, not whole or n < PAIRS - 1
                nb = (b + 1) % BUFS
                k = 0
                for g in range(GROUPS):
                    layer0(n, b, g)
                    if g % 2 == 1 and g // 2 + 2 < CHUNKS:
                        edge(n, b, g // 2 + 2)
                    if has_next and g < 11:
                        for _ in range(3 if g < 6 else 2):
                            ins = x_stats(nb, uses + (1 if nb == 0 else 0), k)
                            k += 1
                        if g == 10:
                            value = link.next()
                            ins.then_inc(dve_step, 1)
                            wait_apart(dve, dve_step, value, dve_passed)
                    if has_x1:
                        if g == 0:
                            x1_moments(n - 1, (b - 1) % BUFS)
                        if g == 1:
                            variance(x1_chain(n - 1), 1, (b - 1) % BUFS)
                        if g == 2:
                            if whole and n == 1:
                                dve.wait_ge(w1_loaded, 32)
                            weights(x1_chain(n - 1), 1, (b - 1) % BUFS)
                        if g == 3:
                            bias(x1_chain(n - 1), 1, (b - 1) % BUFS)
                    if has_next:
                        if g == 10:
                            x_moments()
                            dve.wait_ge(moments_ready, x_chain(n + 1) + 1)
                        if g == 11:
                            variance(x_chain(n + 1), 0, nb)
                            if not whole or n + 2 < PAIRS:
                                next_pair()
                                indices((b + 2) % BUFS)
                        if g == 12:
                            weights(x_chain(n + 1), 0, nb)
                            edge(n + 1, nb, 0)
                        if g == 13:
                            bias(x_chain(n + 1), 0, nb)
                            edge(n + 1, nb, 1)

            in_steps(dve, step, link, LINKS_PER_STEP)
            lb = (PAIRS - 1) % BUFS
            x1_moments(PAIRS - 1, lb)
            variance(x1_chain(PAIRS - 1), 1, lb)
            weights(x1_chain(PAIRS - 1), 1, lb)
            bias(x1_chain(PAIRS - 1), 1, lb)

        @block.tensor
        def _(pe):
            def products(weight, source, g, slot):
                for k in range(2):
                    at = g * GROUP + k * BANK_COLS
                    ins = nc.tensor.matmul(slots[slot][:, k, 0:BANK_COLS], weight, source[:, at:at + BANK_COLS],
                                           start=True, stop=True)
                return ins

            def layer0(n, b, g, free, value):
                if g == 0:
                    pe.wait_ge(weights_ready, x_chain(n) + 1)
                if g % 2 == 0:
                    pe.wait_ge(edges_fixed, n * CHUNKS + (g // 2 + 1))
                if free is not None:
                    pe.wait_ge(free, value)
                products(w0_scaled[:, b, :], shifted, g, layer0_slot(n, b, g)).then_inc(l0_filled, 1)

            def layer1(m, b, g, slot, free, value):
                if g == 0:
                    pe.wait_ge(weights_ready, x1_chain(m) + 1)
                pe.wait_ge(free, value)
                products(w1_scaled[:, b, :], images[b], g, slot).then_inc(l1_filled, 1)

            def stats(number, layer):
                pe.wait_ge(moments_ready, number + 1)
                if not (isinstance(number, int) and number == 0):
                    pe.wait_ge(bias_ready, number)
                nc.tensor.matmul(stats_ps[:, 0:2], group_mean_w, mean_var[:, layer, :], start=True, stop=True)
                nc.tensor.matmul(stats_ps[:, 2:3], group_diff_w, mean_var[:, layer, 0:1],
                                 start=True, stop=True).then_inc(stats_ready, 1)

            def mean_product(number, layer, b):
                pe.wait_ge(weights_ready, number + 1)
                weight = (w0_scaled, w1_scaled)[layer]
                nc.tensor.matmul(mean_ps[:, 0:1], weight[:, b, :], small[:, layer, 0:1],
                                 start=True, stop=True).then_inc(mean_ready, 1)

            pe.wait_ge(consts_loaded, 16 * 5)
            stats(0, 0)
            mean_product(0, 0, 0)

            def step(n, b, uses):
                whole = isinstance(n, int)
                has_x1, has_next = not whole or n > 0, not whole or n < PAIRS - 1
                for g in range(GROUPS):
                    t = n * GROUPS + g
                    if whole and t < SLOTS:
                        layer0(n, b, g, None, 0)
                    elif whole and t <= LAG:
                        layer0(n, b, g, l0_added, t - SLOTS + 1)
                    elif whole and t == LAG + 1:
                        layer0(n, b, g, l0_added, LAG)
                    else:
                        layer0(n, b, g, l1_evacuated, n * GROUPS + (g - LAG - 1))
                    behind(n, b, g, lambda m, mb, mg, slot: layer1(m, mb, mg, slot, l0_added, n * GROUPS + g))
                    if has_x1:
                        if g == 1:
                            stats(x1_chain(n - 1), 1)
                        if g == 3:
                            mean_product(x1_chain(n - 1), 1, (b - 1) % BUFS)
                    if has_next:
                        if g == 11:
                            stats(x_chain(n + 1), 0)
                        if g == 13:
                            mean_product(x_chain(n + 1), 0, (b + 1) % BUFS)

            in_steps(pe, step)
            end = PAIRS * GROUPS
            for t in range(end, end + LAG):
                m, g = divmod(t - LAG, GROUPS)
                if t == end + 1:
                    stats(x1_chain(PAIRS - 1), 1)
                    layer1(m, m % BUFS, g, tail_slot(t), l0_added, end)
                else:
                    layer1(m, m % BUFS, g, tail_slot(t), l1_evacuated, t - LAG - (1 if t == end else 2))
                if t == end + 3:
                    mean_product(x1_chain(PAIRS - 1), 1, (PAIRS - 1) % BUFS)


def _constants():
    eye = np.eye(P, dtype=np.float32)
    swap = eye.reshape(P // 2, 2, P)[:, ::-1].reshape(P, P)
    return np.ascontiguousarray(np.stack([(eye + swap) / 2, (eye - swap) / 2, eye]))


def kernel(**inputs):
    import concourse.bacc as bacc
    from concourse.bass_utils import run_bass_kernel_spmd

    nc = bacc.Bacc("TRN2", target_bir_lowering=False, num_devices=1)
    arrays, args = {}, []
    names = ["x", "L0_conv_weight", "L0_conv_bias", "L0_conv_offsets", "L1_conv_weights"]
    for name in names + ["constants"]:
        a = _constants() if name == "constants" else np.ascontiguousarray(inputs[name])
        arrays[f"in_{name}"] = a
        args.append(nc.dram_tensor(f"in_{name}", a.shape, mybir.dt.from_np(a.dtype), kind="ExternalInput").ap())
    out = nc.dram_tensor("out", (BATCH, C, H, W), mybir.dt.float32, kind="ExternalOutput").ap()
    build(nc, *args, out)
    return run_bass_kernel_spmd(nc, [arrays], core_ids=[0]).results[0]["out"]
```

```python
from contextlib import ExitStack

import concourse.bass as bass
from concourse import mybir
import numpy as np

P = 128
C = 64
BATCH, H, W = 64, 112, 112
HW = H * W
PAIRS = BATCH * C // P
PAIR_ELEMS = P * HW
PAD = 3
HALO = PAD * W + PAD
BANK = 512
GROUP = 2 * BANK
GROUPS = -(-HW // GROUP)
PIECES = -(-HW // BANK)
CHUNK_ROWS = 16
CHUNK = CHUNK_ROWS * W
CHUNKS = HW // CHUNK
SCRATCH = CHUNK + 2 * HALO
LOW_BITS = 8
UNIT = 1 << LOW_BITS
SHIFT_BIAS = 2 * UNIT
BUFS = 3
SLOTS = 3
LAG = 17
FIRST = 2
ROUNDS = (PAIRS - FIRST - 1) // BUFS
LOOP_END = FIRST + ROUNDS * BUFS
LINKS_PER_STEP = 16
EPS = 1e-5
assert HW % UNIT == 0 and CHUNK % UNIT == 0 and FIRST * GROUPS > LAG + 3 and H % CHUNK_ROWS == 0


def span(k, size):
    return slice(k * size, min((k + 1) * size, HW))


def chunks_to(k, size):
    return -(-span(k, size).stop // CHUNK)


def groups_to(j):
    return -(-(j + 1) * CHUNK // GROUP)


class Tally:

    def __init__(self):
        self.count = 0
        self.per_step = 0
        self.inner = 0
        self.step = None

    def enter(self, steps, per_step):
        self.step, self.per_step, self.inner = steps, per_step, 0

    def leave(self, steps):
        assert self.inner == self.per_step, (self.inner, self.per_step)
        self.count += steps * self.per_step
        self.step, self.inner = None, 0

    def next(self):
        if self.step is None:
            self.count += 1
            return self.count
        self.inner += 1
        return self.step * self.per_step + (self.count + self.inner)


def build(nc, x, w0, b0, offsets, w1, consts, out):
    f32, i32 = mybir.dt.float32, mybir.dt.int32
    ALU, ACT, AX = mybir.AluOpType, mybir.ActivationFunctionType, mybir.AxisListType.X

    x_pairs = x.rearrange("b c h w -> (b c) (h w)").rearrange("(n p) f -> n p f", p=P)
    out_pairs = out.rearrange("b c h w -> (b c) (h w)").rearrange("(n p) f -> n p f", p=P)
    x_flat = x.rearrange("b c h w -> (b c h w)").rearrange("(n o) -> n o", o=1)
    head = nc.dram_tensor("head_chunk", (P, SCRATCH), f32, kind="Internal").ap()
    tail = nc.dram_tensor("tail_chunk", (P, SCRATCH), f32, kind="Internal").ap()
    head_flat = head.rearrange("p f -> (p f)").rearrange("(n o) -> n o", o=1)
    tail_flat = tail.rearrange("p f -> (p f)").rearrange("(n o) -> n o", o=1)
    w1_expanded = nc.dram_tensor("w1_expanded", (C, C), f32, kind="Internal").ap()

    with ExitStack() as ctx:
        def sb(name, shape, dt=f32):
            return ctx.enter_context(nc.sbuf_tensor(name, shape, dt))

        def sem(name):
            return ctx.enter_context(nc.semaphore(name))

        images = [sb(f"images{b}", [P, HW]) for b in range(BUFS)]
        shifted = sb("shifted", [P, HW])
        square_out = sb("square_out", [P, GROUP])
        const_sb = sb("const_sb", [P, 4, P])
        group_mean_w, group_diff_w, identity, group_share_w = (const_sb[:, k, :] for k in range(4))
        w0_blocks = sb("w0_blocks", [P, P])
        w1_blocks = sb("w1_blocks", [P, P])
        w0_scaled = sb("w0_scaled", [P, BUFS, P])
        w1_scaled = sb("w1_scaled", [P, BUFS, P])
        bias_in = sb("bias_in", [P, 1])
        bias0 = sb("bias0", [P, BUFS, 1])
        bias1 = sb("bias1", [P, BUFS, 1])
        shift_guess = sb("shift_guess", [P, BUFS, 1])
        group_bias = sb("group_bias", [P, 1])
        bn = sb("bn", [P, PIECES, 6])
        mean_var = sb("mean_var", [P, 2])
        x1_sums = sb("x1_sums", [P, BUFS, 2, GROUPS])
        x1_totals = sb("x1_totals", [P, 2])
        x_stats_g = sb("x_stats_g", [P, BUFS, 3])
        x1_stats_g = sb("x1_stats_g", [P, 2])
        small = sb("small", [P, 2, 5])
        offs = sb("offs", [P, 2], i32)
        offs_f = sb("offs_f", [P, 2])
        flat_shift = sb("flat_shift", [P, 2])
        shift_int = sb("shift_int", [P, 3], i32)
        high = sb("high", [P, CHUNKS], i32)
        scratch_index = sb("scratch_index", [P, 1], i32)
        index = sb("index", [P, BUFS, CHUNKS], i32)
        col_mask = sb("col_mask", [P, 2, PAD], i32)
        row_mask = sb("row_mask", [P, 2, PAD], i32)

        slots = [ctx.enter_context(nc.psum_tensor(f"slot{s}", [P, GROUP], f32)) for s in range(SLOTS)]
        stats_ps = ctx.enter_context(nc.psum_tensor("stats_ps", [P, 512], f32))
        mean_ps = ctx.enter_context(nc.psum_tensor("mean_ps", [P, 512], f32))

        consts_loaded = sem("consts_loaded")
        offsets_loaded = sem("offsets_loaded")
        blocks_zeroed = sem("blocks_zeroed")
        w1_zeroed = sem("w1_zeroed")
        w1_spread = sem("w1_spread")
        w1_loaded = sem("w1_loaded")
        counted = sem("counted")
        head_written, tail_written = sem("head_written"), sem("tail_written")
        x_loaded = [[sem(f"x_loaded{b}_{j}") for j in range(CHUNKS)] for b in range(BUFS)]
        stored = [[sem(f"stored{b}_{j}") for j in range(CHUNKS)] for b in range(BUFS)]
        gathered = [sem(f"gathered{j}") for j in range(CHUNKS)]
        index_ready = sem("index_ready")
        edges_fixed = sem("edges_fixed")
        l0_filled, l1_filled = sem("l0_filled"), sem("l1_filled")
        l0_added, l1_evacuated = sem("l0_added"), sem("l1_evacuated")
        squares_summed = sem("squares_summed")
        moments_ready = sem("moments_ready")
        stats_ready = sem("stats_ready")
        variance_ready = sem("variance_ready")
        root_ready = sem("root_ready")
        weights_ready = sem("weights_ready")
        mean_ready = sem("mean_ready")
        bias_ready = sem("bias_ready")
        masks_ready = sem("masks_ready")
        dve_step = sem("dve_step")

        dve_passed, pool_passed, sp_passed = sem("dve_passed"), sem("pool_passed"), sem("sp_passed")

        def wait_apart(eng, semaphore, value, passed):
            eng.wait_ge(semaphore, value)
            eng.sem_inc(passed, 1)

        def chunk(t, j):
            return t[:, j * CHUNK:(j + 1) * CHUNK]

        def group(t, g):
            return t[:, span(g, GROUP)]

        def products_of(slot, g):
            return slots[slot][:, 0:group(shifted, g).shape[1]]

        def x_chain(n):
            return 0 if isinstance(n, int) and n == 0 else n * 2 - 1

        def x1_chain(n):
            return 2 * PAIRS - 1 if isinstance(n, int) and n == PAIRS - 1 else n * 2 + 2

        def in_steps(eng, step, tally=None, per_step=0):
            for n in range(FIRST):
                step(n, n % BUFS, n // BUFS + 1)
            with eng.Fori(0, ROUNDS) as i:
                for u in range(BUFS):
                    if tally is not None:
                        tally.enter(i * BUFS + u, per_step)
                    n = FIRST + u
                    step(i * BUFS + n, n % BUFS, i + (n // BUFS + 1))
                    if tally is not None:
                        assert tally.inner == per_step, tally.inner
            if tally is not None:
                tally.leave(ROUNDS * BUFS)
            for n in range(LOOP_END, PAIRS):
                step(n, n % BUFS, n // BUFS + 1)

        def behind(n, b, g, do):
            back, at = divmod(g - LAG, GROUPS)
            if isinstance(n, int) and n + back < 0:
                return
            do(n + back, (b + back) % BUFS, at, layer1_slot(n, b, g))

        def layer0_slot(n, b, g):
            if isinstance(n, int) and n * GROUPS + g < LAG:
                return (n * GROUPS + g) % SLOTS
            return (2 * (b * GROUPS + g) - LAG) % SLOTS

        def layer1_slot(n, b, g):
            return (layer0_slot(n, b, g) + 1) % SLOTS

        def tail_slot(t):
            return (2 * PAIRS * GROUPS - LAG + t - PAIRS * GROUPS) % SLOTS

        block = ctx.enter_context(nc.Block())

        @block.sync
        def _(sp):
            sp.dma_start(head[:, HALO:SCRATCH], x_pairs[0, :, 0:CHUNK + HALO]).then_inc(head_written, 16)
            sp.dma_start(head[:, 0:HALO], x_pairs[0, :, 0:HALO]).then_inc(head_written, 16)

            def load(n, b, j):
                sp.dma_start(chunk(images[b], j), x_pairs[n, :, j * CHUNK:(j + 1) * CHUNK]) \
                    .then_inc(x_loaded[b][j], 16)

            for j in range(CHUNKS):
                load(0, 0, j)
            sp.wait_ge(gathered[2], 16)
            for j in range(CHUNKS):
                load(1, 1, j)
            for j in range(CHUNKS):
                sp.wait_ge(l0_filled, groups_to(j))
                load(2, 2, j)
            sp.dma_start(tail[:, 0:CHUNK + HALO], x_pairs[PAIRS - 1, :, HW - CHUNK - HALO:HW]) \
                .then_inc(tail_written, 16)
            sp.dma_start(tail[:, CHUNK + HALO:SCRATCH], x_pairs[PAIRS - 1, :, 0:HALO]).then_inc(tail_written, 16)

            def reload(m, b, uses):
                for j in range(CHUNKS):
                    wait_apart(sp, stored[b][j], uses * 16, sp_passed)
                    load(m + BUFS, b, j)

            reloads = PAIRS - BUFS
            with sp.Fori(0, reloads // BUFS) as i:
                for b in range(BUFS):
                    reload(i * BUFS + b, b, i + 1)
            for m in range(reloads // BUFS * BUFS, reloads):
                reload(m, m % BUFS, m // BUFS + 1)
            for b in range(BUFS):
                for j in range(CHUNKS):
                    sp.wait_ge(stored[b][j], 16 * len(range(b, PAIRS, BUFS)))

        @block.gpsimd
        def _(pool):
            nc.gpsimd.iota(high[:], [[CHUNK // UNIT, CHUNKS]], base=0, channel_multiplier=HW // UNIT)
            nc.gpsimd.iota(scratch_index[:], [[0, 1]], base=HALO, channel_multiplier=SCRATCH).then_inc(counted, 1)

            def gather(source, at, j):
                nc.gpsimd.indirect_dma_start(
                    chunk(shifted, j), None, source,
                    bass.IndirectOffsetOnAxis(ap=at, axis=0)).then_inc(gathered[j], 16)

            pool.wait_ge(index_ready, 1)
            pool.wait_ge(head_written, 32)
            gather(head_flat, scratch_index[:, 0:1], 0)
            for j in range(1, CHUNKS):
                gather(x_flat, index[:, 0, j:j + 1], j)

            def gather_pair(n, b, last=False):
                pool.wait_ge(index_ready, n + 1)
                for j in range(CHUNKS):
                    wait_apart(pool, l0_filled, n * GROUPS + (groups_to(j) - GROUPS), pool_passed)
                    if last and j == CHUNKS - 1:
                        pool.wait_ge(tail_written, 32)
                        gather(tail_flat, scratch_index[:, 0:1], j)
                    else:
                        gather(x_flat, index[:, b, j:j + 1], j)

            rounds = (PAIRS - 2) // BUFS
            with pool.Fori(0, rounds) as i:
                for u in range(BUFS):
                    gather_pair(i * BUFS + (1 + u), (1 + u) % BUFS)
            for n in range(1 + rounds * BUFS, PAIRS):
                gather_pair(n, n % BUFS, n == PAIRS - 1)

        @block.scalar
        def _(act):
            for half in range(2):
                act.dma_start(offs[half * C:(half + 1) * C, :], offsets[:, :]).then_inc(offsets_loaded, 16)
            act.dma_start(const_sb[:], consts.rearrange("k p m -> p k m")).then_inc(consts_loaded, 16)
            act.wait_ge(blocks_zeroed, 1)
            for half in range(2):
                here = slice(half * C, (half + 1) * C)
                act.dma_start(bias_in[here, :], b0.rearrange("(c o) -> c o", o=1)).then_inc(consts_loaded, 16)
                act.dma_start(w0_blocks[here, here], w0[:, :]).then_inc(consts_loaded, 16)
            act.dma_start(w1_expanded[:, :], w1_blocks[0:C, 0:C]).then_inc(w1_zeroed, 16)

            def spread_w1():
                taps = w1.shape[1]
                stride = taps // 2
                turn = C // stride
                w1_taps = w1.rearrange("(q r) j -> r j q", r=turn)
                spread = w1_expanded.rearrange("c (q r) -> r c q", r=turn)
                act.wait_ge(w1_zeroed, 16)
                with nc.allow_non_contiguous_dma(reason="single weights, once"):
                    for r in range(turn):
                        inside = min(taps, C - stride * r)
                        act.dma_start(spread[r, stride * r:stride * r + inside, :], w1_taps[r, 0:inside, :]) \
                            .then_inc(w1_spread, 16)
                        if inside < taps:
                            act.dma_start(spread[r, 0:taps - inside, :], w1_taps[r, inside:taps, :]) \
                                .then_inc(w1_spread, 16)
                return turn + 1

            def load_w1(spreads):
                act.wait_ge(w1_spread, 16 * spreads)
                for half in range(2):
                    here = slice(half * C, (half + 1) * C)
                    act.dma_start(w1_blocks[here, here], w1_expanded[:, :]).then_inc(w1_loaded, 16)

            def square(n, b, g):
                act.wait_ge(l0_added, n * GROUPS + (g + 1))
                if not (isinstance(n, int) and n == 0 and g == 0):
                    act.wait_ge(squares_summed, n * GROUPS + g)
                x1 = group(images[b], g)
                nc.scalar.activation(square_out[:, 0:x1.shape[1]], x1, ACT.Square, bias=shift_guess[:, b, :],
                                     accum_out=x1_sums[:, b, 1, g:g + 1]).then_inc(squares_summed, 1)

            def layer1(m, b, g, slot):
                if g == 0:
                    act.wait_ge(bias_ready, x1_chain(m) + 1)
                act.wait_ge(l1_filled, m * GROUPS + (g + 1))
                nc.scalar.activation(group(images[b], g), products_of(slot, g), ACT.Identity,
                                     bias=bias1[:, b, :]).then_inc(l1_evacuated, 1)
                for j in range(CHUNKS):
                    if groups_to(j) == g + 1:
                        act.wait_ge(l1_evacuated, m * GROUPS + (g + 1))
                        act.dma_start(out_pairs[m, :, j * CHUNK:(j + 1) * CHUNK], chunk(images[b], j)) \
                            .then_inc(stored[b][j], 16)

            def root(number, layer):
                act.wait_ge(variance_ready, number + 1)
                nc.scalar.activation(small[:, layer, 2:3], small[:, layer, 1:2], ACT.Sqrt).then_inc(root_ready, 1)

            root(0, 0)
            spreads = spread_w1()

            def step(n, b, uses):
                for g in range(GROUPS):
                    if g > 0:
                        square(n, b, g - 1)
                    elif not (isinstance(n, int) and n == 0):
                        square(n - 1, (b - 1) % BUFS, GROUPS - 1)
                    behind(n, b, g, layer1)
                    if g == GROUPS - 2 and isinstance(n, int) and n == 0:
                        load_w1(spreads)
                    if g == 1 and not (isinstance(n, int) and n == 0):
                        root(x1_chain(n - 1), 1)
                    if g == 10 and not (isinstance(n, int) and n == PAIRS - 1):
                        root(x_chain(n + 1), 0)

            in_steps(act, step)
            square(PAIRS - 1, (PAIRS - 1) % BUFS, GROUPS - 1)
            for t in range(PAIRS * GROUPS, PAIRS * GROUPS + LAG):
                if t == PAIRS * GROUPS + 1:
                    root(x1_chain(PAIRS - 1), 1)
                m, g = divmod(t - LAG, GROUPS)
                layer1(m, m % BUFS, g, tail_slot(t))

        @block.vector
        def _(dve):
            link = Tally()

            def then(ins):
                value = link.next()
                ins.then_inc(dve_step, 1)
                dve.wait_ge(dve_step, value)

            V = nc.vector
            V.memset(w0_blocks[:], 0.0)
            V.memset(w1_blocks[:], 0.0).then_inc(blocks_zeroed, 1)

            dve.wait_ge(offsets_loaded, 32)
            then(V.tensor_copy(offs_f[:], offs[:]))
            then(V.tensor_scalar(flat_shift[:, 0:1], offs_f[:, 0:1], float(W), float(SHIFT_BIAS), ALU.mult, ALU.add))
            then(V.tensor_tensor(shift_int[:, 0:1], flat_shift[:, 0:1], offs_f[:, 1:2], ALU.add))
            then(V.tensor_scalar(shift_int[:, 1:2], shift_int[:, 0:1], UNIT - 1, None, ALU.bitwise_and))
            then(V.tensor_scalar(shift_int[:, 2:3], shift_int[:, 0:1], LOW_BITS, None, ALU.logical_shift_right))
            dve.wait_ge(counted, 1)
            then(V.tensor_scalar(high[:], high[:], shift_int[:, 2:3], float(-(SHIFT_BIAS // UNIT)),
                                 ALU.add, ALU.add))
            then(V.tensor_scalar(scratch_index[:], scratch_index[:], shift_int[:, 0:1], float(-SHIFT_BIAS),
                                 ALU.add, ALU.add))

            def indices(b):
                V.tensor_scalar(index[:, b, :], high[:], LOW_BITS, shift_int[:, 1:2],
                                ALU.logical_shift_left, ALU.bitwise_or).then_inc(index_ready, 1)

            def next_pair():
                then(V.tensor_scalar(high[:], high[:], float(PAIR_ELEMS // UNIT), None, ALU.add))

            indices(0)
            next_pair()
            indices(1)
            for axis, mask in ((0, row_mask), (1, col_mask)):
                for k in range(PAD):
                    V.tensor_scalar(mask[:, 0, k:k + 1], offs_f[:, axis:axis + 1], float(k), 0.0,
                                    ALU.add, ALU.is_lt)
                    last = V.tensor_scalar(mask[:, 1, k:k + 1], offs_f[:, axis:axis + 1], float(k), float(PAD - 1),
                                           ALU.add, ALU.is_gt)
            last.then_inc(masks_ready, 1)

            def x_stats(b, uses, k):
                if k == 0 or chunks_to(k, BANK) > chunks_to(k - 1, BANK):
                    dve.wait_ge(x_loaded[b][chunks_to(k, BANK) - 1], uses * 16)
                return V.bn_stats(bn[:, k, :], images[b][:, span(k, BANK)])

            def x_moments():
                V.bn_aggr(mean_var[:], bn[:].rearrange("p k s -> p (k s)")).then_inc(moments_ready, 1)

            def x_variance(number, b):
                s, stats = small[:, 0, :], x_stats_g[:, b, :]
                dve.wait_ge(stats_ready, number + 1)
                then(V.tensor_copy(stats, stats_ps[:, 0:3]))
                V.scalar_tensor_tensor(shift_guess[:, b, :], stats[:, 0:1], -1.0, group_bias[:],
                                       ALU.mult, ALU.subtract)
                then(V.tensor_scalar(s[:, 0:1], stats[:, 2:3], stats[:, 2:3], EPS, ALU.mult, ALU.add))
                V.tensor_tensor(s[:, 1:2], s[:, 0:1], stats[:, 1:2], ALU.add).then_inc(variance_ready, 1)

            def x1_moments(n, b):
                dve.wait_ge(squares_summed, n * GROUPS + GROUPS)
                V.reduce_sum(x1_totals[:], x1_sums[:, b, :, :], AX).then_inc(moments_ready, 1)

            def x1_variance(number, b):
                s = small[:, 1, :]
                dve.wait_ge(stats_ready, number + 1)
                then(V.tensor_copy(x1_stats_g[:], stats_ps[:, 0:2]))
                then(V.tensor_tensor(s[:, 0:1], x1_stats_g[:, 0:1], shift_guess[:, b, :], ALU.add))
                then(V.scalar_tensor_tensor(s[:, 4:5], s[:, 0:1], s[:, 0:1], x1_stats_g[:, 1:2],
                                            ALU.mult, ALU.subtract))
                V.tensor_scalar(s[:, 1:2], s[:, 4:5], -1.0, EPS, ALU.mult, ALU.add).then_inc(variance_ready, 1)

            def weights(number, layer, b):
                s = small[:, layer, :]
                dve.wait_ge(root_ready, number + 1)
                then(V.reciprocal(s[:, 0:1], s[:, 2:3]))
                then(V.scalar_tensor_tensor(s[:, 3:4], s[:, 0:1], s[:, 1:2], s[:, 0:1], ALU.mult, ALU.mult))
                then(V.tensor_scalar(s[:, 4:5], s[:, 3:4], -0.5, 1.5, ALU.mult, ALU.add))
                if layer == 0:
                    V.tensor_scalar(w0_scaled[:, b, :], w0_blocks[:], s[:, 0:1], s[:, 4:5], ALU.mult, ALU.mult) \
                        .then_inc(weights_ready, 1)
                else:
                    then(V.tensor_tensor(s[:, 3:4], s[:, 0:1], s[:, 4:5], ALU.mult))
                    V.scalar_tensor_tensor(w1_scaled[:, b, :], w1_blocks[:], s[:, 3:4], identity,
                                           ALU.mult, ALU.add).then_inc(weights_ready, 1)

            def bias(number, layer, b):
                dve.wait_ge(mean_ready, number + 1)
                if layer == 0:
                    ins = V.tensor_tensor(bias0[:, b, :], bias_in[:], mean_ps[:, 0:1], ALU.subtract)
                else:
                    ins = V.tensor_tensor(bias1[:, b, :], x1_stats_g[:, 0:1], mean_ps[:, 0:1], ALU.subtract)
                ins.then_inc(bias_ready, 1)
                if layer == 0:
                    dve.wait_ge(bias_ready, number + 1)

            def edge(n, b, j):
                wait_apart(dve, gathered[j], n * 16 + 16, dve_passed)
                mean = x_stats_g[:, b, 0:1].unsqueeze(2)
                if j == 0 or j == CHUNKS - 1:
                    side = 0 if j == 0 else 1
                    at = 0 if j == 0 else HW - PAD * W
                    rows = shifted[:, at:at + PAD * W].rearrange("p (h w) -> p h w", w=W)
                    value = link.next()
                    V.copy_predicated(rows, row_mask[:, side, :].unsqueeze(2).to_broadcast([P, PAD, W]),
                                      mean.to_broadcast([P, PAD, W])).then_inc(dve_step, 1)
                    wait_apart(dve, dve_step, value, dve_passed)
                columns = bass.AP(tensor=shifted, offset=j * CHUNK,
                                  ap=[[HW, P], [W, CHUNK_ROWS], [W - PAD, 2], [1, PAD]])
                V.copy_predicated(
                    columns, col_mask[:].unsqueeze(1).to_broadcast([P, CHUNK_ROWS, 2, PAD]),
                    mean.unsqueeze(3).to_broadcast([P, CHUNK_ROWS, 2, PAD])).then_inc(edges_fixed, 1)

            def layer0(n, b, g):
                dve.wait_ge(l0_filled, n * GROUPS + (g + 1))
                V.scalar_tensor_tensor(group(images[b], g), products_of(layer0_slot(n, b, g), g),
                                       bias0[:, b, :], group(images[b], g), ALU.add, ALU.add,
                                       accum_out=x1_sums[:, b, 0, g:g + 1]).then_inc(l0_added, 1)

            dve.wait_ge(masks_ready, 1)
            for k in range(PIECES):
                ins = x_stats(0, 1, k)
            then(ins)
            dve.wait_ge(consts_loaded, 16 * 5)
            x_moments()
            dve.wait_ge(stats_ready, 1)
            V.tensor_copy(group_bias[:], stats_ps[:, 3:4])
            x_variance(0, 0)
            weights(0, 0, 0)
            edge(0, 0, 0)
            bias(0, 0, 0)
            edge(0, 0, 1)

            def step(n, b, uses):
                whole = isinstance(n, int)
                has_x1, has_next = not whole or n > 0, not whole or n < PAIRS - 1
                before, after = (b - 1) % BUFS, (b + 1) % BUFS
                k = 0
                for g in range(GROUPS):
                    layer0(n, b, g)
                    if g > 0:
                        for j in range(chunks_to(g - 1, GROUP), chunks_to(g, GROUP)):
                            if j + 1 < CHUNKS:
                                edge(n, b, j + 1)
                    if has_next and g < 10:
                        for _ in range(3 if g < 5 else 2):
                            ins = x_stats(after, uses + (1 if after == 0 else 0), k)
                            k += 1
                        if g == 9:
                            assert k == PIECES
                            value = link.next()
                            ins.then_inc(dve_step, 1)
                            wait_apart(dve, dve_step, value, dve_passed)
                            x_moments()
                    if has_x1:
                        if g == 0:
                            x1_moments(n - 1, before)
                        if g == 1:
                            x1_variance(x1_chain(n - 1), before)
                        if g == 2:
                            if whole and n == 1:
                                dve.wait_ge(w1_loaded, 32)
                            weights(x1_chain(n - 1), 1, before)
                        if g == 3:
                            bias(x1_chain(n - 1), 1, before)
                    if has_next:
                        if g == 10:
                            x_variance(x_chain(n + 1), after)
                            if not whole or n + 2 < PAIRS:
                                next_pair()
                                indices((b + 2) % BUFS)
                        if g == 11:
                            weights(x_chain(n + 1), 0, after)
                            edge(n + 1, after, 0)
                        if g == 12:
                            bias(x_chain(n + 1), 0, after)
                            edge(n + 1, after, 1)

            in_steps(dve, step, link, LINKS_PER_STEP)
            lb = (PAIRS - 1) % BUFS
            x1_moments(PAIRS - 1, lb)
            x1_variance(x1_chain(PAIRS - 1), lb)
            weights(x1_chain(PAIRS - 1), 1, lb)
            bias(x1_chain(PAIRS - 1), 1, lb)

        @block.tensor
        def _(pe):
            def products(weight, source, g, slot):
                into, from_ = products_of(slot, g), group(source, g)
                columns = into.shape[1]
                for at in range(0, columns, BANK):
                    bank = slice(at, min(at + BANK, columns))
                    ins = nc.tensor.matmul(into[:, bank], weight, from_[:, bank],
                                           start=True, stop=True)
                return ins

            def layer0(n, b, g, free, value):
                if g == 0:
                    pe.wait_ge(weights_ready, x_chain(n) + 1)
                if g == 0 or chunks_to(g, GROUP) > chunks_to(g - 1, GROUP):
                    pe.wait_ge(edges_fixed, n * CHUNKS + chunks_to(g, GROUP))
                if free is not None:
                    pe.wait_ge(free, value)
                products(w0_scaled[:, b, :], shifted, g, layer0_slot(n, b, g)).then_inc(l0_filled, 1)

            def layer1(m, b, g, slot, free, value):
                if g == 0:
                    pe.wait_ge(weights_ready, x1_chain(m) + 1)
                pe.wait_ge(free, value)
                products(w1_scaled[:, b, :], images[b], g, slot).then_inc(l1_filled, 1)

            def x_group_stats(number):
                pe.wait_ge(moments_ready, number + 1)
                if not (isinstance(number, int) and number == 0):
                    pe.wait_ge(bias_ready, number)
                nc.tensor.matmul(stats_ps[:, 0:2], group_mean_w, mean_var[:], start=True, stop=True)
                nc.tensor.matmul(stats_ps[:, 2:3], group_diff_w, mean_var[:, 0:1],
                                 start=True, stop=True).then_inc(stats_ready, 1)

            def x1_group_stats(number):
                pe.wait_ge(moments_ready, number + 1)
                pe.wait_ge(bias_ready, number)
                nc.tensor.matmul(stats_ps[:, 0:2], group_share_w, x1_totals[:],
                                 start=True, stop=True).then_inc(stats_ready, 1)

            def mean_product(number, layer, b):
                pe.wait_ge(weights_ready, number + 1)
                weight, mean = ((w0_scaled[:, b, :], x_stats_g[:, b, 0:1]),
                                (w1_scaled[:, b, :], x1_stats_g[:, 0:1]))[layer]
                nc.tensor.matmul(mean_ps[:, 0:1], weight, mean, start=True, stop=True).then_inc(mean_ready, 1)

            pe.wait_ge(consts_loaded, 16 * 5)
            nc.tensor.matmul(stats_ps[:, 3:4], group_mean_w, bias_in[:], start=True, stop=True)
            x_group_stats(0)
            mean_product(0, 0, 0)

            def step(n, b, uses):
                whole = isinstance(n, int)
                has_x1, has_next = not whole or n > 0, not whole or n < PAIRS - 1
                for g in range(GROUPS):
                    t = n * GROUPS + g
                    if whole and t < SLOTS:
                        layer0(n, b, g, None, 0)
                    elif whole and t <= LAG:
                        layer0(n, b, g, l0_added, t - SLOTS + 1)
                    elif whole and t == LAG + 1:
                        layer0(n, b, g, l0_added, LAG)
                    else:
                        layer0(n, b, g, l1_evacuated, n * GROUPS + (g - LAG - 1))
                    behind(n, b, g, lambda m, mb, mg, slot: layer1(m, mb, mg, slot, l0_added, n * GROUPS + g))
                    if has_x1:
                        if g == 1:
                            x1_group_stats(x1_chain(n - 1))
                        if g == 3:
                            mean_product(x1_chain(n - 1), 1, (b - 1) % BUFS)
                    if has_next:
                        if g == 10:
                            x_group_stats(x_chain(n + 1))
                        if g == 12:
                            mean_product(x_chain(n + 1), 0, (b + 1) % BUFS)

            in_steps(pe, step)
            end = PAIRS * GROUPS
            for t in range(end, end + LAG):
                m, g = divmod(t - LAG, GROUPS)
                if t == end + 1:
                    x1_group_stats(x1_chain(PAIRS - 1))
                    layer1(m, m % BUFS, g, tail_slot(t), l0_added, end)
                else:
                    layer1(m, m % BUFS, g, tail_slot(t), l1_evacuated, t - LAG - (1 if t == end else 2))
                if t == end + 3:
                    mean_product(x1_chain(PAIRS - 1), 1, (PAIRS - 1) % BUFS)


def _constants():
    eye = np.eye(P, dtype=np.float32)
    swap = eye.reshape(P // 2, 2, P)[:, ::-1].reshape(P, P)
    return np.ascontiguousarray(np.stack([(eye + swap) / 2, (eye - swap) / 2, eye, (eye + swap) / (2 * HW)])
                                .astype(np.float32))


def kernel(**inputs):
    import concourse.bacc as bacc
    from concourse.bass_utils import run_bass_kernel_spmd

    nc = bacc.Bacc("TRN2", target_bir_lowering=False, num_devices=1)
    arrays, args = {}, []
    names = ["x", "L0_conv_weight", "L0_conv_bias", "L0_conv_offsets", "L1_conv_weights"]
    for name in names + ["constants"]:
        a = _constants() if name == "constants" else np.ascontiguousarray(inputs[name])
        arrays[f"in_{name}"] = a
        args.append(nc.dram_tensor(f"in_{name}", a.shape, mybir.dt.from_np(a.dtype), kind="ExternalInput").ap())
    out = nc.dram_tensor("out", (BATCH, C, H, W), mybir.dt.float32, kind="ExternalOutput").ap()
    build(nc, *args, out)
    return run_bass_kernel_spmd(nc, [arrays], core_ids=[0]).results[0]["out"]
```
